# Optimizing a Trainium2 kernel written in Bass

```python
import numpy as np
import jax
import jax.numpy as jnp

def _softmax(x, axis=-1):
    return jax.nn.softmax(x, axis=axis)

def _gelu(x):
    return jax.nn.gelu(x, approximate=True)

def _silu(x):
    return jax.nn.silu(x)

def _sigmoid(x):
    return jax.nn.sigmoid(x)

def _layernorm(x, axis=-1, eps=1e-05):
    m = jnp.mean(x, axis=axis, keepdims=True)
    v = jnp.var(x, axis=axis, keepdims=True)
    return (x - m) / jnp.sqrt(v + eps)

def _scatter_add(tgt, idx, src, axis=0):
    return tgt.at[idx].add(src)

def _segment_sum(src, seg, n):
    return jax.ops.segment_sum(src, seg, n)
kernel_name = 'mk_gnn_preln_d4_gnn_r16_3c1c4b'

def setup_inputs(seed: int=0):
    np.random.seed(seed)
    _w = jnp.asarray

    def _rec_inputs():
        import jax
        import jax.numpy as jnp
        _gk = jax.random.key(seed)
        x = -0.000202 + 1 * jax.random.normal(jax.random.fold_in(_gk, 1), (3125, 128), jnp.float32)
        src = jax.random.randint(jax.random.fold_in(_gk, 2), (100000,), 0, 3125, jnp.int32)
        dst = jnp.minimum((3125 * jax.random.uniform(jax.random.fold_in(_gk, 3), (100000,)) ** 2.0).astype(jnp.int32), 49999)
        _o = jnp.argsort(dst, stable=True)
        src = src[_o]
        dst = dst[_o]
        edge_type_16 = jax.random.randint(jax.random.fold_in(_gk, 13), (100000,), 0, 16, jnp.int32)
        edge_weight = jax.random.uniform(jax.random.fold_in(_gk, 14), (100000,), jnp.float32, 0.0, 1)
        return (x, src, dst, edge_type_16, edge_weight)
    x, src, dst, edge_type_16, edge_weight = _rec_inputs()

    def _L0_gnn_setup():
        import jax, jax.numpy as jnp
        import numpy as np
        N = 3125
        E = 50000
        IN = 128
        OUT = 128
        H = 4
        C = OUT // H
        NEG_SLOPE = 0.2

        def gat_layer(x, W, a_s, a_d, b, src, dst):
            h = (x @ W).reshape(-1, H, C)
            al_src = jnp.einsum('nhc,hc->nh', h, a_s)
            al_dst = jnp.einsum('nhc,hc->nh', h, a_d)
            e = jax.nn.leaky_relu(al_src[src] + al_dst[dst], NEG_SLOPE)
            m = jax.ops.segment_max(e, dst, num_segments=N)
            m = jnp.where(jnp.isfinite(m), m, 0.0)
            w = jnp.exp(e - m[dst])
            denom = jax.ops.segment_sum(w, dst, num_segments=N)
            alpha = w / jnp.maximum(denom[dst], 1e-16)
            msg = h[src] * alpha[:, :, None]
            out = jax.ops.segment_sum(msg, dst, num_segments=N)
            return out.reshape(-1, H * C) + b
        key = jax.random.key(seed)
        ks = jax.random.split(key, 11)
        x = jax.random.normal(ks[0], (N, IN), dtype=jnp.float32)
        edge_index = jax.random.randint(ks[1], (2, E), 0, N, dtype=jnp.int64)
        W1 = jax.random.normal(ks[2], (IN, H * C), dtype=jnp.float32) / np.sqrt(IN)
        a_src1 = jax.random.normal(ks[3], (H, C), dtype=jnp.float32) / np.sqrt(C)
        a_dst1 = jax.random.normal(ks[4], (H, C), dtype=jnp.float32) / np.sqrt(C)
        b1 = jnp.zeros((H * C,), dtype=jnp.float32)
        W2 = jax.random.normal(ks[5], (OUT, H * C), dtype=jnp.float32) / np.sqrt(OUT)
        a_src2 = jax.random.normal(ks[6], (H, C), dtype=jnp.float32) / np.sqrt(C)
        a_dst2 = jax.random.normal(ks[7], (H, C), dtype=jnp.float32) / np.sqrt(C)
        b2 = jnp.zeros((H * C,), dtype=jnp.float32)
        return {'x': x, 'edge_index': edge_index, 'W1': W1, 'a_src1': a_src1, 'a_dst1': a_dst1, 'b1': b1, 'W2': W2, 'a_src2': a_src2, 'a_dst2': a_dst2, 'b2': b2}
    _L0_gnn_all = _L0_gnn_setup()
    _L0_gnn_in = {k: v for k, v in _L0_gnn_all.items() if k in ('W1', 'a_src1', 'a_dst1', 'b1', 'W2', 'a_src2', 'a_dst2', 'b2')}
    del _L0_gnn_all

    def _L1_gnn_setup():
        import jax, jax.numpy as jnp
        import numpy as np
        N = 3125
        F = 128
        D = 128
        K = 4
        E = 50000
        EPS = 1e-12
        key = jax.random.key(seed)
        k1, k2, k3, k4, k5 = jax.random.split(key, 5)
        x = jax.random.normal(k1, (N, F), dtype=jnp.float32)
        edge_vals = jax.random.uniform(k2, (E,), dtype=jnp.float32)
        weights = jax.random.normal(k3, (K, F, D), dtype=jnp.float32) * 0.05
        edge_row = jax.random.randint(k4, (E,), 0, N, dtype=jnp.int32)
        edge_col = jax.random.randint(k5, (E,), 0, N, dtype=jnp.int32)
        return {'x': x, 'edge_vals': edge_vals, 'weights': weights, 'edge_row': edge_row, 'edge_col': edge_col}
    _L1_gnn_all = _L1_gnn_setup()
    _L1_gnn_in = {k: v for k, v in _L1_gnn_all.items() if k in ('weights',)}
    del _L1_gnn_all

    def _L2_gnn_setup():
        import jax, jax.numpy as jnp
        import numpy as np
        N = 6250
        E = 100000
        DIN, DH, DE_ = (128, 128, 128)
        EPS = 1e-05

        def _layer_norm(h, g, b):
            mu = jnp.mean(h, axis=-1, keepdims=True)
            var = jnp.mean(jnp.square(h - mu), axis=-1, keepdims=True)
            return (h - mu) * jax.lax.rsqrt(var + EPS) * g + b

        def _prelu(h, a):
            return jnp.where(h > 0, h, a * h)
        key = jax.random.key(seed)
        ks = jax.random.split(key, 24)
        rn = lambda k, s, sc=0.05: jax.random.normal(k, s, dtype=jnp.float32) * sc
        return {'x': rn(ks[0], (N, DIN), 1.0), 'src': jax.random.randint(ks[1], (E,), 0, N), 'dst': jax.random.randint(ks[2], (E,), 0, N), 'Wself1': rn(ks[3], (DIN, DH)), 'Wneigh1': rn(ks[4], (DIN, DH)), 'b1': jnp.zeros((DH,), jnp.float32), 'Wself2': rn(ks[5], (DH, DH)), 'Wneigh2': rn(ks[6], (DH, DH)), 'b2': jnp.zeros((DH,), jnp.float32), 'Wself3': rn(ks[7], (DH, DE_)), 'Wneigh3': rn(ks[8], (DH, DE_)), 'b3': jnp.zeros((DE_,), jnp.float32), 'Wskip1': rn(ks[9], (DIN, DH)), 'Wskip2': rn(ks[10], (DIN, DH)), 'g1': jnp.ones((DH,), jnp.float32), 'beta1': jnp.zeros((DH,), jnp.float32), 'g2': jnp.ones((DH,), jnp.float32), 'beta2': jnp.zeros((DH,), jnp.float32), 'g3': jnp.ones((DE_,), jnp.float32), 'beta3': jnp.zeros((DE_,), jnp.float32), 'a1': jnp.float32(0.25), 'a2': jnp.float32(0.25), 'a3': jnp.float32(0.25)}
    _L2_gnn_all = _L2_gnn_setup()
    _L2_gnn_in = {k: v for k, v in _L2_gnn_all.items() if k in ('Wself1', 'Wneigh1', 'b1', 'Wself2', 'Wneigh2', 'b2', 'Wself3', 'Wneigh3', 'b3', 'Wskip1', 'Wskip2', 'g1', 'beta1', 'g2', 'beta2', 'g3', 'beta3', 'a1', 'a2', 'a3')}
    del _L2_gnn_all

    def _L3_gnn_setup():
        import jax, jax.numpy as jnp
        import numpy as np
        N, H = (3125, 128)
        E = 50000
        ETD = 32
        NUM_ET = 16
        LN_EPS = 1e-05
        key = jax.random.key(seed)
        ks = jax.random.split(key, 9)
        x = jax.random.normal(ks[0], (N, H), dtype=jnp.float32)
        edge_index = jax.random.randint(ks[1], (2, E), 0, N, dtype=jnp.int64)
        edge_type = jax.random.randint(ks[2], (E,), 0, NUM_ET, dtype=jnp.int64)
        edge_emb_W = jax.random.normal(ks[3], (NUM_ET, ETD), dtype=jnp.float32)
        lim_msg = 1.0 / np.sqrt(H + ETD)
        msg_W = jax.random.uniform(ks[4], (H, H + ETD), jnp.float32, -lim_msg, lim_msg)
        msg_b = jax.random.uniform(ks[5], (H,), jnp.float32, -lim_msg, lim_msg)
        lim_upd = 1.0 / np.sqrt(H)
        upd_W = jax.random.uniform(ks[6], (H, H), jnp.float32, -lim_upd, lim_upd)
        upd_b = jax.random.uniform(ks[7], (H,), jnp.float32, -lim_upd, lim_upd)
        ln_g = jnp.ones((H,), jnp.float32)
        ln_b = jnp.zeros((H,), jnp.float32)
        return {'x': x, 'edge_index': edge_index, 'edge_type': edge_type, 'edge_emb_W': edge_emb_W, 'msg_W': msg_W, 'msg_b': msg_b, 'upd_W': upd_W, 'upd_b': upd_b, 'ln_g': ln_g, 'ln_b': ln_b}
    _L3_gnn_all = _L3_gnn_setup()
    _L3_gnn_in = {k: v for k, v in _L3_gnn_all.items() if k in ('edge_emb_W', 'msg_W', 'msg_b', 'upd_W', 'upd_b', 'ln_g', 'ln_b')}
    del _L3_gnn_all
    return {'x': x, 'src': src, 'dst': dst, 'edge_type_16': edge_type_16, 'edge_weight': edge_weight, 'L0_gnn_W1': _L0_gnn_in['W1'], 'L0_gnn_a_src1': _L0_gnn_in['a_src1'], 'L0_gnn_a_dst1': _L0_gnn_in['a_dst1'], 'L0_gnn_b1': _L0_gnn_in['b1'], 'L0_gnn_W2': _L0_gnn_in['W2'], 'L0_gnn_a_src2': _L0_gnn_in['a_src2'], 'L0_gnn_a_dst2': _L0_gnn_in['a_dst2'], 'L0_gnn_b2': _L0_gnn_in['b2'], 'L1_gnn_weights': _L1_gnn_in['weights'], 'L2_gnn_Wself1': _L2_gnn_in['Wself1'], 'L2_gnn_Wneigh1': _L2_gnn_in['Wneigh1'], 'L2_gnn_b1': _L2_gnn_in['b1'], 'L2_gnn_Wself2': _L2_gnn_in['Wself2'], 'L2_gnn_Wneigh2': _L2_gnn_in['Wneigh2'], 'L2_gnn_b2': _L2_gnn_in['b2'], 'L2_gnn_Wself3': _L2_gnn_in['Wself3'], 'L2_gnn_Wneigh3': _L2_gnn_in['Wneigh3'], 'L2_gnn_b3': _L2_gnn_in['b3'], 'L2_gnn_Wskip1': _L2_gnn_in['Wskip1'], 'L2_gnn_Wskip2': _L2_gnn_in['Wskip2'], 'L2_gnn_g1': _L2_gnn_in['g1'], 'L2_gnn_beta1': _L2_gnn_in['beta1'], 'L2_gnn_g2': _L2_gnn_in['g2'], 'L2_gnn_beta2': _L2_gnn_in['beta2'], 'L2_gnn_g3': _L2_gnn_in['g3'], 'L2_gnn_beta3': _L2_gnn_in['beta3'], 'L2_gnn_a1': _L2_gnn_in['a1'], 'L2_gnn_a2': _L2_gnn_in['a2'], 'L2_gnn_a3': _L2_gnn_in['a3'], 'L3_gnn_edge_emb_W': _L3_gnn_in['edge_emb_W'], 'L3_gnn_msg_W': _L3_gnn_in['msg_W'], 'L3_gnn_msg_b': _L3_gnn_in['msg_b'], 'L3_gnn_upd_W': _L3_gnn_in['upd_W'], 'L3_gnn_upd_b': _L3_gnn_in['upd_b'], 'L3_gnn_ln_g': _L3_gnn_in['ln_g'], 'L3_gnn_ln_b': _L3_gnn_in['ln_b']}

def reference(x, src, dst, edge_type_16, edge_weight, L0_gnn_W1, L0_gnn_a_src1, L0_gnn_a_dst1, L0_gnn_b1, L0_gnn_W2, L0_gnn_a_src2, L0_gnn_a_dst2, L0_gnn_b2, L1_gnn_weights, L2_gnn_Wself1, L2_gnn_Wneigh1, L2_gnn_b1, L2_gnn_Wself2, L2_gnn_Wneigh2, L2_gnn_b2, L2_gnn_Wself3, L2_gnn_Wneigh3, L2_gnn_b3, L2_gnn_Wskip1, L2_gnn_Wskip2, L2_gnn_g1, L2_gnn_beta1, L2_gnn_g2, L2_gnn_beta2, L2_gnn_g3, L2_gnn_beta3, L2_gnn_a1, L2_gnn_a2, L2_gnn_a3, L3_gnn_edge_emb_W, L3_gnn_msg_W, L3_gnn_msg_b, L3_gnn_upd_W, L3_gnn_upd_b, L3_gnn_ln_g, L3_gnn_ln_b):
    import jax
    import jax.numpy as jnp

    def _L0_gnn_ref(x, edge_index, W1, a_src1, a_dst1, b1, W2, a_src2, a_dst2, b2):
        import jax, jax.numpy as jnp
        import numpy as np
        N = 3125
        E = 50000
        IN = 128
        OUT = 128
        H = 4
        C = OUT // H
        NEG_SLOPE = 0.2

        def gat_layer(x, W, a_s, a_d, b, src, dst):
            h = (x @ W).reshape(-1, H, C)
            al_src = jnp.einsum('nhc,hc->nh', h, a_s)
            al_dst = jnp.einsum('nhc,hc->nh', h, a_d)
            e = jax.nn.leaky_relu(al_src[src] + al_dst[dst], NEG_SLOPE)
            m = jax.ops.segment_max(e, dst, num_segments=N)
            m = jnp.where(jnp.isfinite(m), m, 0.0)
            w = jnp.exp(e - m[dst])
            denom = jax.ops.segment_sum(w, dst, num_segments=N)
            alpha = w / jnp.maximum(denom[dst], 1e-16)
            msg = h[src] * alpha[:, :, None]
            out = jax.ops.segment_sum(msg, dst, num_segments=N)
            return out.reshape(-1, H * C) + b
        loop = jnp.arange(N, dtype=edge_index.dtype)
        src = jnp.concatenate([edge_index[0], loop])
        dst = jnp.concatenate([edge_index[1], loop])
        x = jax.nn.relu(gat_layer(x, W1, a_src1, a_dst1, b1, src, dst))
        x = jax.nn.relu(gat_layer(x, W2, a_src2, a_dst2, b2, src, dst))
        return x

    def _L1_gnn_ref(x, edge_vals, weights, edge_row, edge_col):
        import jax, jax.numpy as jnp
        import numpy as np
        N = 3125
        F = 128
        D = 128
        K = 4
        E = 50000
        EPS = 1e-12
        n = x.shape[0]
        k = weights.shape[0]

        def spmv(v):
            return jax.ops.segment_sum(edge_vals[:, None] * v[edge_col], edge_row, num_segments=n)
        v0 = x * jax.lax.rsqrt(jnp.maximum(jnp.sum(x * x, axis=0, keepdims=True), EPS))

        def step(carry, _):
            v_prev, v_prev2, beta_prev = carry
            w = spmv(v_prev)
            alpha = jnp.sum(w * v_prev, axis=0, keepdims=True)
            new_v = w - alpha * v_prev - beta_prev * v_prev2
            beta = jnp.sqrt(jnp.sum(new_v * new_v, axis=0, keepdims=True))
            v = new_v / beta
            return ((v, v_prev, beta), v)
        init = (v0, jnp.zeros_like(v0), jnp.zeros((1, x.shape[1]), x.dtype))
        _, vs = jax.lax.scan(step, init, None, length=k - 1)
        Vs = jnp.concatenate([v0[None], vs], axis=0)
        out = jnp.einsum('knf,kfd->nd', Vs, weights)
        return jax.nn.relu(out)

    def _L2_gnn_ref(x, src, dst, Wself1, Wneigh1, b1, Wself2, Wneigh2, b2, Wself3, Wneigh3, b3, Wskip1, Wskip2, g1, beta1, g2, beta2, g3, beta3, a1, a2, a3):
        import jax, jax.numpy as jnp
        import numpy as np
        N = 6250
        E = 100000
        DIN, DH, DE_ = (128, 128, 128)
        EPS = 1e-05

        def _layer_norm(h, g, b):
            mu = jnp.mean(h, axis=-1, keepdims=True)
            var = jnp.mean(jnp.square(h - mu), axis=-1, keepdims=True)
            return (h - mu) * jax.lax.rsqrt(var + EPS) * g + b

        def _prelu(h, a):
            return jnp.where(h > 0, h, a * h)
        n = x.shape[0]
        deg = jax.ops.segment_sum(jnp.ones((src.shape[0],), jnp.float32), dst, num_segments=n)
        inv_deg = 1.0 / jnp.maximum(deg, 1.0)

        def sage(h, Ws, Wn, b):
            agg = jax.ops.segment_sum(h[src], dst, num_segments=n) * inv_deg[:, None]
            return h @ Ws + agg @ Wn + b
        h1 = _prelu(_layer_norm(sage(x, Wself1, Wneigh1, b1), g1, beta1), a1)
        h2 = _prelu(_layer_norm(sage(h1 + x @ Wskip1, Wself2, Wneigh2, b2), g2, beta2), a2)
        ret = _prelu(_layer_norm(sage(h1 + h2 + x @ Wskip2, Wself3, Wneigh3, b3), g3, beta3), a3)
        return ret

    def _L3_gnn_ref(x, edge_index, edge_type, edge_emb_W, msg_W, msg_b, upd_W, upd_b, ln_g, ln_b):
        import jax, jax.numpy as jnp
        import numpy as np
        N, H = (3125, 128)
        E = 50000
        ETD = 32
        NUM_ET = 16
        LN_EPS = 1e-05
        src = edge_index[0]
        dst = edge_index[1]
        et = edge_emb_W[edge_type]
        m_in = jnp.concatenate([x[src], et], axis=-1)
        m = jax.nn.relu(m_in @ msg_W.T + msg_b)
        agg = jax.ops.segment_sum(m, dst, num_segments=x.shape[0])
        deg = jax.ops.segment_sum(jnp.ones_like(dst, dtype=x.dtype), dst, num_segments=x.shape[0])
        agg = agg / jnp.clip(deg, 1.0)[:, None]
        out = agg @ upd_W.T + upd_b
        h = x + out
        mu = jnp.mean(h, axis=-1, keepdims=True)
        var = jnp.mean((h - mu) ** 2, axis=-1, keepdims=True)
        return (h - mu) * jax.lax.rsqrt(var + LN_EPS) * ln_g + ln_b
    edge_index = jnp.stack([src, dst])
    h = jnp.maximum(_layernorm(x, axis=-1), 0.0)
    x = x + _L0_gnn_ref(h, edge_index, L0_gnn_W1, L0_gnn_a_src1, L0_gnn_a_dst1, L0_gnn_b1, L0_gnn_W2, L0_gnn_a_src2, L0_gnn_a_dst2, L0_gnn_b2)
    h = jnp.maximum(_layernorm(x, axis=-1), 0.0)
    x = x + _L1_gnn_ref(h, edge_weight, L1_gnn_weights, src, dst)
    h = jnp.maximum(_layernorm(x, axis=-1), 0.0)
    x = x + _L2_gnn_ref(h, src, dst, L2_gnn_Wself1, L2_gnn_Wneigh1, L2_gnn_b1, L2_gnn_Wself2, L2_gnn_Wneigh2, L2_gnn_b2, L2_gnn_Wself3, L2_gnn_Wneigh3, L2_gnn_b3, L2_gnn_Wskip1, L2_gnn_Wskip2, L2_gnn_g1, L2_gnn_beta1, L2_gnn_g2, L2_gnn_beta2, L2_gnn_g3, L2_gnn_beta3, L2_gnn_a1, L2_gnn_a2, L2_gnn_a3)
    h = jnp.maximum(_layernorm(x, axis=-1), 0.0)
    x = x + _L3_gnn_ref(h, edge_index, edge_type_16, L3_gnn_edge_emb_W, L3_gnn_msg_W, L3_gnn_msg_b, L3_gnn_upd_W, L3_gnn_upd_b, L3_gnn_ln_g, L3_gnn_ln_b)
    return x

_drawn_inputs = setup_inputs


def setup_inputs(seed=0):
    import zlib

    import numpy as np

    out = dict(_drawn_inputs(seed))
    spreads = {'L0_gnn_b1': (0.0, 0.1),
     'L0_gnn_b2': (0.0, 0.1),
     'L2_gnn_b1': (0.0, 0.1),
     'L2_gnn_b2': (0.0, 0.1),
     'L2_gnn_b3': (0.0, 0.1),
     'L2_gnn_g1': (1.0, 0.2),
     'L2_gnn_beta1': (0.0, 0.1),
     'L2_gnn_g2': (1.0, 0.2),
     'L2_gnn_beta2': (0.0, 0.1),
     'L2_gnn_g3': (1.0, 0.2),
     'L2_gnn_beta3': (0.0, 0.1),
     'L3_gnn_ln_g': (1.0, 0.2),
     'L3_gnn_ln_b': (0.0, 0.1)}
    factors = {'edge_weight': 21.544,
     'L0_gnn_a_dst1': 64.0,
     'L0_gnn_a_src2': 36.613,
     'L0_gnn_a_dst2': 64.0,
     'L1_gnn_weights': 5.4,
     'L3_gnn_edge_emb_W': 2.785,
     'L3_gnn_msg_b': 4.443}
    for name, (base, spread) in spreads.items():
        noise = np.random.default_rng([zlib.crc32(name.encode()), seed]).standard_normal(out[name].shape)
        drawn = base * np.exp(spread * noise) if base else spread * noise
        out[name] = jnp.asarray(drawn.astype(out[name].dtype))
    for name, factor in factors.items():
        out[name] = (out[name] * factor).astype(out[name].dtype)
    return out
```

```python
from contextlib import ExitStack

import concourse.bass as bass
from concourse import mybir

F32 = mybir.dt.float32
I32 = mybir.dt.int32
ALU = mybir.AluOpType
ACT = mybir.ActivationFunctionType
AX = mybir.AxisListType

N = 3125
D = 128
E = 100000
HEADS = 4
HC = D // HEADS
TYPES = 16
TP = 125
NT = N // TP
CH = 7
CW = 448
NP = CH * CW
EC = E // TP
NPAIR = EC // 2
JUNK = 2 * TP
ABSENT = -1e30
assert TP * NT == N and NP >= N and EC % 4 == 0 and NT == 1 + 3 * 7 + 3


class Order:

    def __init__(self, eng, sem):
        self.eng, self.sem, self.n, self.off = eng, sem, 0, 0

    def __call__(self, ins):
        ins.then_inc(self.sem, 1)
        self.n += 1
        self.eng.wait_ge(self.sem, self.n + self.off)


def sweep(eng, n, body):
    def at(t):
        return (NT * n + t) % 3, (NT * n + t) // 3
    body(0, *at(0))
    with eng.Fori(0, 7) as i:
        for u in range(3):
            slot, turn = at(1 + u)
            body(i * 3 + (1 + u), slot, i + turn)
    for t in range(22, NT):
        body(t, *at(t))


def pairs(eng, body, order=None, steps=0):
    body(0, 0, True)
    body(1, 1, True)
    start = order.n if order else 0
    with eng.Fori(1, NPAIR // 2) as i:
        for u in range(2):
            if order:
                order.off = (i - 1) * (2 * steps)
            body(i * 2 + u, u, False)
    if order:
        assert order.n == start + 2 * steps
        order.n, order.off = start + 2 * steps * (NPAIR // 2 - 1), 0


def graph_layers(nc, x, src, dst, etype, eweight, W1, as1, ad1, b1, W2, as2, ad2, b2, LW,
                 Wself1, Wneigh1, sb1, Wself2, Wneigh2, sb2, Wself3, Wneigh3, sb3, Wskip1, Wskip2,
                 g1, beta1, g2, beta2, g3, beta3, a1, a2, a3, embW, msgW, msgb, updW, updb, lng, lnb,
                 out):
    with ExitStack() as ctx:
        def sb(name, shape, dt=F32):
            return ctx.enter_context(nc.sbuf_tensor(name, shape, dt))

        sems = {}

        def S(name):
            if name not in sems:
                sems[name] = ctx.enter_context(nc.semaphore(name))
            return sems[name]

        count_d = nc.dram_tensor("edge_count", [N * NP + JUNK, 1], F32).ap()
        weight_d = nc.dram_tensor("edge_weight_sum", [N * NP + JUNK, 1], F32).ap()
        count_m = count_d[0:N * NP, :].rearrange("(n d) o -> n (d o)", d=NP)
        weight_m = weight_d[0:N * NP, :].rearrange("(n d) o -> n (d o)", d=NP)
        table_d = nc.dram_tensor("message_table", [TYPES * N, D], F32).ap()
        agg_d = nc.dram_tensor("message_sum", [N + JUNK, D], F32).ap()

        fm = sb("feature_major", [128, 9 * NP])

        def arr(k):
            return fm[:, k * NP:(k + 1) * NP]

        X, Dinv, H, Sf, Df, P0, P1, P2, P3 = (arr(k) for k in range(9))
        seg = fm[0:TP, 5 * NP:9 * NP].rearrange("p (h n) -> p h n", h=HEADS)
        tiles = sb("tiles", [128, 3 * NP])
        A = [tiles[0:TP, s * NP:(s + 1) * NP] for s in range(3)]
        NM = sb("node_major", [TP, NT, D])
        hs = sb("stationary_tile", [TP, 3, D])
        edges = sb("edges", [TP, 3, EC], I32)
        srcI, dstI, typeI = (edges[:, k, :] for k in range(3))
        mats = {}
        consts = sb("consts", [128, 26 * 128])

        def mat(name):
            if name not in mats:
                k = len(mats)
                assert k < 26
                mats[name] = consts[:, k * 128:(k + 1) * 128]
            return mats[name]

        cols = sb("columns", [128, 64])
        col_at = {}

        def col(name):
            if name not in col_at:
                col_at[name] = len(col_at)
                assert len(col_at) <= 64
            return cols[:, col_at[name]:col_at[name] + 1]

        s8 = sb("s8", [TP, NT * HEADS])
        s2 = sb("s2", [TP, NT * HEADS])
        s1 = sb("s1", [TP, NT * HEADS])
        smax = sb("smax", [TP, NT, HEADS])
        ident, mean_m, ones_m, block_m = mat("ident"), mat("mean"), mat("ones"), mat("block")
        junk_i = sb("junk_i", [TP, 4], I32)
        junk_f = sb("junk_f", [TP, 4])

        U = [tiles[0:TP, s * 1792:(s + 1) * 1792].rearrange("p (h n) -> p h n", h=HEADS) for s in range(3)]
        B = [tiles[0:TP, 5376 + s * CW:5376 + (s + 1) * CW] for s in range(3)]
        hp = [tiles[0:TP, 6720 + s * 512:6720 + (s + 1) * 512].rearrange("p (g n) -> p g n", g=2)
              for s in range(3)]
        smaxD = tiles[0:TP, 0:NT * D]
        accs = tiles[:, 8256:8256 + 2 * CW].rearrange("p (g n) -> p g n", g=2)
        rows = fm[0:TP, 3 * NP:3 * NP + 4 * 1792].rearrange("p (s k h n) -> p s k h n", s=2, k=2, h=HEADS)

        e0 = 5 * NP
        keyF = fm[0:TP, e0:e0 + EC]
        junkD = fm[0:TP, e0 + EC:e0 + 2 * EC]
        wF = fm[0:TP, e0 + 2 * EC:e0 + 3 * EC]
        e1 = e0 + 3 * EC
        eq = fm[0:TP, e1:e1 + 1000].rearrange("p (s a n) -> p s a n", s=2, a=2)
        eqo = fm[0:TP, e1 + 1000:e1 + 1250]
        msg = fm[0:TP, e1 + 1280:e1 + 1280 + 512].rearrange("p (s a n) -> p s a n", s=2, a=2)
        summed = fm[0:TP, e1 + 1792:e1 + 1792 + 512].rearrange("p (s a n) -> p s a n", s=2, a=2)
        gidx = fm[0:TP, e1 + 2304:e1 + 2304 + EC + 4].bitcast(I32)
        keyW = fm[0:TP, e1 + 3112:e1 + 3112 + EC]
        junkW = fm[0:TP, e1 + 3912:e1 + 3912 + EC]
        earlier = sb("earlier", [TP, 2, 2 * TP])
        ks = sb("key_slot", [TP, 2, 2])
        ws = sb("value_slot", [TP, 2, 2, 2])
        vs = sb("sum_slot", [TP, 2, 2, 2])
        dup = sb("repeats", [TP, 2, 2])
        jk = sb("junk_step", [TP, 2, 2])
        idx = sb("target", [TP, 2, 2], I32)
        jkw = sb("junk_step_w", [TP, 2, 2])
        idxw = sb("target_w", [TP, 2, 2], I32)
        gs = sb("gather_index", [TP, 2, 2], I32)
        TR = fm[0:TP, 3 * NP:3 * NP + TYPES * D].rearrange("p (k n) -> p k n", k=TYPES)
        tab = [tiles[0:TP, s * NT * D:(s + 1) * NT * D].rearrange("p (t n) -> p t n", t=NT) for s in range(2)]

        LN = [(X, Sf, Df, Df), (X, P2, P3, P3), (X, P2, P3, P3), (P1, P2, P3, P3), (P1, P2, P3, P3),
              (P1, P2, P3, P3), (X, P2, P3, P3), (P1, P2, P3, P3)]
        V = [H, Sf, Df, P0]
        SIN = [H, Df, Sf]
        NM_ATT, NM_V, NM_S, NM_MSG, NM_LAST = [1, 2], [3, 4, 5], [6, 7, 8], 9, 10
        SEG_ALL = [HEADS * NT * (k + 1) + 3 * HEADS for k in range(2)]

        BIG = ctx.enter_context(nc.psum_tensor("BIG", [128, CH, 512], F32))
        SM = ctx.enter_context(nc.psum_tensor("SM", [128, 512], F32))
        big = BIG[:, :, 0:CW]
        bigT = BIG[:, :, :].rearrange("p b (q n) -> p (b q) n", n=128)

        def ch(a):
            return a.rearrange("p (b n) -> p b n", b=CH)

        loads = [("W1", W1), ("W2", W2)] + [(f"LW{k}", LW[k]) for k in range(4)] + [
            ("Wself1", Wself1), ("Wneigh1", Wneigh1), ("Wself2", Wself2), ("Wneigh2", Wneigh2),
            ("Wself3", Wself3), ("Wneigh3", Wneigh3), ("Wskip1", Wskip1), ("Wskip2", Wskip2),
            ("msgx", msgW[:, 0:D]), ("updW", updW)]
        vec = [("as1", as1), ("ad1", ad1), ("b1", b1), ("as2", as2), ("ad2", ad2), ("b2", b2),
               ("sb1", sb1), ("sb2", sb2), ("sb3", sb3), ("g1", g1), ("g2", g2), ("g3", g3),
               ("beta1", beta1), ("beta2", beta2), ("beta3", beta3), ("updb", updb),
               ("lng", lng), ("lnb", lnb)]
        msge = sb("msge", [128, 32])
        msgb_row = sb("msgb_row", [1, D])
        emb = sb("emb", [TYPES, 32])
        embT = sb("embT", [32, TYPES])
        for n, _ in loads:
            mat(n)
        asel, adel, selA, selB, denA, denB = (mat(n) for n in ("asel", "adel", "selA", "selB", "denA", "denB"))
        pick = sb("pick", [128, HEADS, TP])
        weT = sb("weT", [32, D])
        n_loads = len(loads) + len(vec) + 3 + 3 + 3

        block = ctx.enter_context(nc.Block())

        @block.sync
        def _(sp):
            sp.dma_start(NM[:, :, :], x.rearrange("(t p) n -> p t n", p=TP)).then_inc(S("x_loaded"), 16)
            for n, a in loads:
                sp.dma_start(mat(n), a).then_inc(S("params"), 16)
            for n, a in vec:
                a = a if len(a.shape) == 1 else a.rearrange("h c -> (h c)")
                sp.dma_start(col(n), a.rearrange("(p o) -> p o", o=1)).then_inc(S("params"), 16)
            for n, a in (("a1", a1), ("a2", a2), ("a3", a3)):
                sp.dma_start(col(n), a.rearrange("(o k) -> o k", o=1).to_broadcast([128, 1])).then_inc(S("params"), 16)
            sp.dma_start(msge[:, :], msgW[:, D:D + 32]).then_inc(S("params"), 16)
            sp.dma_start(msgb_row[:, :], msgb.rearrange("(o p) -> o p", o=1)).then_inc(S("params"), 16)
            sp.dma_start(emb[:, :], embW).then_inc(S("params"), 16)
            for k, a in enumerate((src, dst, etype)):
                sp.dma_start(edges[:, k, :], a.rearrange("(p c) -> p c", p=TP)).then_inc(S("params"), 16)
            sp.dma_start(wF, eweight.rearrange("(p c) -> p c", p=TP)).then_inc(S("weights_loaded"), 16)
            sp.wait_ge(S("zero_tile"), 1)
            with sp.Fori(0, NT) as t:
                sp.dma_start(count_m[bass.ds(t * TP, TP), :], A[0]).then_inc(S("cleared"), 16)
                sp.dma_start(weight_m[bass.ds(t * TP, TP), :], A[0]).then_inc(S("cleared"), 16)
            for m in (count_d, weight_d):
                sp.dma_start(m[N * NP:, :].rearrange("(p o) n -> p (o n)", p=TP), A[0][:, 0:2]).then_inc(S("cleared"), 16)
            for k in range(0, (N + JUNK) // TP):
                sp.dma_start(agg_d[k * TP:(k + 1) * TP, :], A[0][:, 0:D]).then_inc(S("cleared"), 16)

            def stream(matrix, k):
                def body(t, s, turn):
                    if k < 2:
                        sp.wait_ge(S("seg_step"), t * HEADS + (HEADS * NT * k + HEADS))
                    else:
                        sp.wait_ge(S("tile_free"), t + (NT * (k - 2) + 1))
                    sp.dma_start(A[s], matrix[bass.ds(t * TP, TP), :] if not isinstance(t, int)
                                 else matrix[t * TP:(t + 1) * TP, :]).then_inc(S(f"tile_in{s}"), 16)
                sweep(sp, k, body)

            def attention(layer):
                for q in range(CH):
                    base = 25 * (CH * layer + q)

                    def body(t, s, turn):
                        sp.wait_ge(S("w_made"), t + (base + 1))
                        rows_t = bass.ds(t * TP, TP) if not isinstance(t, int) else slice(t * TP, (t + 1) * TP)
                        sp.dma_start(B[s], count_m[rows_t, q * CW:(q + 1) * CW]).then_inc(S(f"block_in{s}"), 16)
                    sweep(sp, CH * layer + q, body)

            sp.wait_ge(S("count_done"), 1)
            k = 0
            for layer in range(2):
                if layer:
                    sp.wait_ge(S("attended"), 1 * CH)
                stream(count_m, k)
                k += 1
                sp.wait_ge(S("seg_step"), SEG_ALL[layer])
                attention(layer)
            sp.wait_ge(S("attended"), 2 * CH)
            for j in range(3):
                stream(weight_m, k)
                k += 1
            for j in range(3):
                stream(count_m, k)
                k += 1
            for j in range(TYPES):
                sp.wait_ge(S("table_made"), j + 1)
                sp.dma_start(table_d[j * N:(j + 1) * N, :].rearrange("(t p) n -> p t n", p=TP),
                             tab[j % 2]).then_inc(S(f"table_out{j % 2}"), 16)
            sp.wait_ge(S("messages_done"), 1)
            sp.dma_start(NM[:, :, :], agg_d[0:N, :].rearrange("(t p) n -> p t n", p=TP)).then_inc(S("agg_loaded"), 16)
            sp.wait_ge(S("nm_ready"), NM_LAST)
            sp.dma_start(out.rearrange("(t p) n -> p t n", p=TP), NM[:, :, :]).then_inc(S("out_written"), 16)
            sp.wait_ge(S("out_written"), 16)

        @block.gpsimd
        def _(pool):
            o = Order(pool, S("pool_order"))
            o(nc.gpsimd.memset(A[0], 0.0))
            pool.nop().then_inc(S("zero_tile"), 1)
            o(nc.gpsimd.memset(ones_m, 1.0))
            o(nc.gpsimd.memset(mean_m, 1.0 / D))
            for m in (ident, selA, selB, denA, denB, block_m):
                o(nc.gpsimd.memset(m, 0.0))
            o(nc.gpsimd.memset(pick[:, :, :], 0.0))
            o(nc.gpsimd.memset(X[:, N:NP], 0.0))
            o(nc.gpsimd.memset(ws[:, :, :, :], 1.0))
            o(nc.gpsimd.memset(col("eps5"), 1e-5))
            o(nc.gpsimd.memset(earlier[:, :, :], 1.0))
            o(nc.gpsimd.memset(earlier[:, 0, TP:2 * TP], 0.0))
            o(nc.gpsimd.affine_select(out=ident, in_=ident, compare_op=ALU.not_equal, fill=1.0,
                                      base=0, pattern=[[-1, 128]], channel_multiplier=1))
            for a in range(2):
                cut = earlier[:, a, a * TP:(a + 1) * TP]
                o(nc.gpsimd.affine_select(out=cut, in_=cut, compare_op=ALU.is_gt, fill=0.0, base=0,
                                          pattern=[[-1, TP]], channel_multiplier=1))
            for h in range(HEADS):
                r = slice(HC * h, HC * (h + 1))
                o(nc.gpsimd.memset(block_m[r, r], 1.0))
                o(nc.gpsimd.memset(pick[HC * h:HC * h + 1, h, :], 1.0))
            for g, (sel, den) in enumerate(((selA, denA), (selB, denB))):
                for e in range(2):
                    f = slice(64 * g + HC * e, 64 * g + HC * e + HC)
                    o(nc.gpsimd.tensor_copy(sel[64 * e:64 * e + HC, f], ident[64 * e:64 * e + HC, 64 * e:64 * e + HC]))
                    o(nc.gpsimd.memset(den[64 * e + HC:64 * e + HC + 1, f], 1.0))
            o(nc.gpsimd.iota(junk_i[:, 0:2], pattern=[[TP, 2]], base=N * NP, channel_multiplier=1))
            o(nc.gpsimd.iota(junk_i[:, 2:4], pattern=[[TP, 2]], base=N, channel_multiplier=1))
            pool.nop().then_inc(S("consts_made"), 1)

            pool.wait_ge(S("cleared"), 16 * (2 * NT + 2 + (N + JUNK) // TP))

            def scatter(i, s, first):
                pool.wait_ge(S("edge_index"), i + 1)
                pool.wait_ge(S("edge_sums"), i + 1)
                for m, to, c, sem in ((weight_d, idxw, 0, "weights_added"), (count_d, idx, 1, "counts_added")):
                    if not (first and s == 0):
                        pool.wait_ge(S(sem), i * 32)
                    pool.nop(nofuse=True)
                    for a in range(2):
                        nc.gpsimd.indirect_dma_start(
                            out=m, out_offset=bass.IndirectOffsetOnAxis(ap=to[:, s, a:a + 1], axis=0),
                            in_=vs[:, s, a, c:c + 1], in_offset=None, bounds_check=N * NP + JUNK - 1,
                            compute_op=ALU.add).then_inc(S(sem), 16)
            pairs(pool, scatter)
            pool.wait_ge(S("counts_added"), 32 * NPAIR)
            pool.wait_ge(S("weights_added"), 32 * NPAIR)
            pool.nop().then_inc(S("count_done"), 1)

            for layer in range(2):
                def body(t, s, turn):
                    pool.wait_ge(S(f"tile_in{s}"), (turn + 1) * 16)
                    if layer == 0:
                        pool.wait_ge(S("deg_used"), t + 1)
                    pool.nop(nofuse=True)
                    nc.gpsimd.tensor_scalar(A[s], A[s], 0.5, ABSENT, ALU.is_lt, ALU.mult).then_inc(S("mask_made"), 1)
                sweep(pool, layer, body)
                pool.wait_ge(S("seg_step"), SEG_ALL[layer])
                for s in range(3):
                    o(nc.gpsimd.memset(hp[s], 0.0))
                    for e in range(2):
                        o(nc.gpsimd.memset(hp[s][:, :, 192 * e + HC:192 * e + HC + 1], 1.0))
                pool.wait_ge(S("nm_ready"), NM_ATT[layer])
                for q in range(CH):
                    base = 25 * (CH * layer + q)

                    def body(t, s, turn):
                        pool.wait_ge(S("hp_free"), t + (base + 1))
                        pool.nop(nofuse=True)
                        t_nm = NM[:, t, :] if isinstance(t, int) else NM[:, bass.ds(t, 1), :].rearrange("p o n -> p (o n)")
                        v = t_nm.rearrange("p (g e n) -> p g e n", g=2, e=2)
                        for e in range(2):
                            nc.gpsimd.tensor_copy(hp[s][:, :, 192 * e:192 * e + HC], v[:, :, e, :]).then_inc(S("hp_made"), 1)
                    sweep(pool, CH * layer + q, body)

            pool.wait_ge(S("table_out0"), 16 * (TYPES // 2))
            pool.wait_ge(S("table_out1"), 16 * (TYPES // 2))

            def gather(i, s):
                for a in range(2):
                    nc.gpsimd.indirect_dma_start(
                        out=msg[:, s, a, :], out_offset=None, in_=table_d,
                        in_offset=bass.IndirectOffsetOnAxis(ap=gs[:, s, a:a + 1], axis=0)).then_inc(S(f"gathered{s}"), 16)

            pool.wait_ge(S("gather_index"), 1)
            gather(0, 0)

            def messages(i, s, first):
                pool.wait_ge(S("gather_index"), i + 2)
                if not (first and s == 0):
                    pool.wait_ge(S("msg_used"), i)
                pool.nop(nofuse=True)
                gather(i + 1, 1 - s)
                pool.wait_ge(S("msg_index"), i + 1)
                pool.wait_ge(S("msg_sums"), i + 1)
                if not (first and s == 0):
                    pool.wait_ge(S("messages_added"), i * 32)
                pool.nop(nofuse=True)
                for a in range(2):
                    nc.gpsimd.indirect_dma_start(
                        out=agg_d, out_offset=bass.IndirectOffsetOnAxis(ap=idx[:, s, a:a + 1], axis=0),
                        in_=summed[:, s, a, :], in_offset=None, bounds_check=N + JUNK - 1,
                        compute_op=ALU.add).then_inc(S("messages_added"), 16)
            pairs(pool, messages)
            pool.wait_ge(S("messages_added"), 32 * NPAIR)
            pool.wait_ge(S("gathered0"), 32 * (NPAIR // 2 + 1))
            pool.nop().then_inc(S("messages_done"), 1)

        @block.tensor
        def _(pe):
            pe.nop().then_inc(S("tile_free"), 3)
            pe.nop().then_inc(S("hp_free"), 3)

            def mm(out_ap, lhsT, rhs, start=True, stop=True):
                return nc.tensor.matmul(out_ap, lhsT, rhs, start=start, stop=stop)

            def product(terms, sources_ready, done):
                for sem, v in sources_ready:
                    pe.wait_ge(S(sem), v)
                for b in range(CH):
                    for j, (w, a) in enumerate(terms):
                        last = mm(big[:, b, :], w, a[:, b * CW:(b + 1) * CW], j == 0, j == len(terms) - 1)
                last.then_inc(S(done), 1)

            def layer_norm(k):
                src_arr = LN[k][0]
                product([(mean_m, src_arr)], [("ln_in", k + 1)], "ln_mean")
                product([(mean_m, LN[k][3])], [("ln_square", k + 1)], "ln_var")

            def to_node_major(a, ready):
                for sem, v in ready:
                    pe.wait_ge(S(sem), v)
                for t in range(NT):
                    last = nc.tensor.transpose(bigT[0:TP, t, :], a[:, t * TP:(t + 1) * TP], ident)
                last.then_inc(S("turned"), 1)

            def to_feature_major(ready):
                for sem, v in ready:
                    pe.wait_ge(S(sem), v)
                for t in range(NT):
                    last = nc.tensor.transpose(BIG[:, t // 4, (t % 4) * TP:(t % 4 + 1) * TP], NM[:, t, :], ident[0:TP, 0:TP])
                last.then_inc(S("fm_turned"), 1)

            def keys_to_rows(s):
                for a in range(2):
                    last = nc.tensor.transpose(SM[0:TP, a * TP:(a + 1) * TP],
                                               ks[:, s, a:a + 1].to_broadcast([TP, TP]), ident[0:TP, 0:TP])
                return last

            def aggregate(j):
                k = 2 + j

                def body(t, s, turn):
                    pe.wait_ge(S(f"tile_in{s}"), (turn + 1) * 16)
                    pe.wait_ge(S("hs_ready"), t + (25 * j + 1))
                    first, stop = isinstance(t, int) and t == 0, isinstance(t, int) and t == NT - 1
                    for b in range(CH):
                        last = mm(big[:, b, :], hs[:, s, :], A[s][:, b * CW:(b + 1) * CW], first, stop)
                    last.then_inc(S("tile_free"), 1)
                sweep(pe, k, body)

            pe.wait_ge(S("consts_made"), 1)
            pe.wait_ge(S("params"), 16 * n_loads)
            to_feature_major([("x_loaded", 16)])
            for layer in range(2):
                W = mat("W1") if layer == 0 else mat("W2")
                if layer == 0:
                    layer_norm(0)
                product([(W, H if layer == 0 else P1)], [("gat_in", 1) if layer == 0 else ("attended", CH)], "gat_h")
                product([(asel, H)], [("gat_h_copied", layer + 1), ("gat_sel", layer + 1)], "gat_s")
                product([(adel, H)], [("gat_s_copied", layer + 1)], "gat_d")
                to_node_major(Sf, [("gat_d_copied", layer + 1)])
                to_node_major(H, [("s_cols", layer + 1)])
                if layer == 0:
                    def build(i, s, first):
                        pe.wait_ge(S("edge_slot"), i * 2 + 2)
                        if not (first and s == 0):
                            pe.wait_ge(S("edge_eq"), i * 2)
                        keys_to_rows(s).then_inc(S("key_rows"), 1)
                        pe.wait_ge(S("edge_eq"), i * 2 + 2)
                        if not (first and s == 0):
                            pe.wait_ge(S("edge_sums"), i)
                        for a in range(2):
                            for b in range(2):
                                last = mm(SM[0:TP, 256 + 2 * a:258 + 2 * a], eq[:, s, b, a * TP:(a + 1) * TP],
                                          ws[:, s, b, :], b == 0, b == 1)
                        last.then_inc(S("edge_summed"), 1)
                    pairs(pe, build)

                    pe.wait_ge(S("nm_ready"), NM_ATT[0])

                    def degree(t, s, turn):
                        pe.wait_ge(S(f"tile_in{s}"), (turn + 1) * 16)
                        first, stop = isinstance(t, int) and t == 0, isinstance(t, int) and t == NT - 1
                        for b in range(CH):
                            last = mm(big[:, b, :], ones_m[0:TP, :], A[s][:, b * CW:(b + 1) * CW], first, stop)
                        last.then_inc(S("deg_used"), 1)
                    sweep(pe, 0, degree)
                    pe.wait_ge(S("deg_read"), 1)
                pe.wait_ge(S("seg_step"), SEG_ALL[layer])
                pe.wait_ge(S("nm_ready"), NM_ATT[layer])
                for t in range(NT):
                    if t >= CH:
                        pe.wait_ge(S("smax_made"), NT * layer + t - CH + 1)
                    for h in range(HEADS):
                        last = nc.tensor.transpose(BIG[0:TP, t % CH, h * TP:(h + 1) * TP],
                                                   seg[:, h, t * TP:(t + 1) * TP], ident[0:TP, 0:TP])
                    last.then_inc(S("seg_turned"), 1)
                pe.wait_ge(S("smax_spread"), layer + 1)
                for t in range(NT):
                    last = nc.tensor.transpose(BIG[:, t // 4, (t % 4) * TP:(t % 4 + 1) * TP],
                                               smaxD[:, t * D:(t + 1) * D],
                                               ident[0:TP, 0:TP])
                last.then_inc(S("smax_turned"), 1)

                def make_rows(q):
                    for k, a in enumerate((P1, P2)):
                        for h in range(HEADS):
                            n = ((layer * CH + q) * 2 + k) * HEADS + h
                            if n >= 2:
                                pe.wait_ge(S("row_copied"), n - 1)
                            mm(BIG[0:TP, 4 + h % 2, 0:CW], pick[:, h, :], a[:, q * CW:(q + 1) * CW]).then_inc(S("row_made"), 1)

                pe.wait_ge(S("gat_rows"), layer + 1)
                make_rows(0)
                for q in range(CH):
                    if q + 1 < CH:
                        make_rows(q + 1)
                    base = 25 * (CH * layer + q)

                    def body(t, s, turn):
                        pe.wait_ge(S("hp_made"), t * 2 + (2 * base + 2))
                        pe.wait_ge(S("w_made"), t + (base + 4))
                        first, stop = isinstance(t, int) and t == 0, isinstance(t, int) and t == NT - 1
                        for h in range(HEADS):
                            g, e = h // 2, h % 2
                            last = mm(BIG[:, g, 0:CW], hp[s][:, g, e * 128:(e + 1) * 128], U[s][:, h, :],
                                      first and e == 0, stop and e == 1)
                        last.then_inc(S("hp_free"), 1)
                    sweep(pe, CH * layer + q, body)
                    pe.wait_ge(S("acc_copied"), layer * CH + q + 1)
                    mm(BIG[:, 2, 0:CW], selA, accs[:, 0, :], True, False)
                    mm(BIG[:, 2, 0:CW], selB, accs[:, 1, :], False, True)
                    mm(BIG[:, 3, 0:CW], denA, accs[:, 0, :], True, False)
                    mm(BIG[:, 3, 0:CW], denB, accs[:, 1, :], False, True).then_inc(S("att_placed"), 1)
            pe.wait_ge(S("attended"), 2 * CH)
            layer_norm(1)
            for j in range(3):
                to_node_major(V[j], [("v_ready", j + 1)])
                pe.wait_ge(S("nm_ready"), NM_V[j])
                aggregate(j)
                pe.wait_ge(S("agg_read"), j + 1)
            product([(mat(f"LW{k}"), V[k]) for k in range(4)], [("v_ready", 4)], "lanczos_out")
            layer_norm(2)
            for j in range(3):
                if j:
                    product([(mat(f"Wskip{j}"), H)], [("sage_prev", j)], "skip")
                to_node_major(SIN[j], [("sage_in", j + 1)])
                pe.wait_ge(S("nm_ready"), NM_S[j])
                aggregate(3 + j)
                product([(mat(f"Wself{j + 1}"), SIN[j]), (mat(f"Wneigh{j + 1}"), P0)], [("sage_agg", j + 1)], "sage_out")
                layer_norm(3 + j)
            layer_norm(6)
            pe.wait_ge(S("h3_ready"), 1)
            nc.tensor.transpose(BIG[:, 0, 0:128], mat("msgx"), ident)
            nc.tensor.transpose(BIG[:, 1, 0:128], mat("updW"), ident)
            nc.tensor.transpose(BIG[0:32, 2, 0:128], msge[:, :], ident)
            nc.tensor.transpose(BIG[0:32, 3, 0:TYPES], emb[:, :], ident[0:TYPES, 0:TYPES]).then_inc(S("w_turned"), 1)
            pe.wait_ge(S("w_copied"), 1)
            for t in range(NT):
                last = mm(bigT[0:TP, t, :], H[:, t * TP:(t + 1) * TP], asel)
            last.then_inc(S("msg_x"), 1)
            pe.wait_ge(S("nm_ready"), NM_MSG)
            for k in range(TYPES):
                mm(bigT[0:TP, k, :], embT[:, k:k + 1].to_broadcast([32, TP]), weT[:, :], True, False)
                last = mm(bigT[0:TP, k, :], ones_m[0:1, 0:TP], msgb_row[:, :], False, True)
            last.then_inc(S("msg_t"), 1)

            def messages(i, s, first):
                pe.wait_ge(S("msg_slot"), i + 1)
                if not (first and s == 0):
                    pe.wait_ge(S("msg_eq"), i * 2)
                keys_to_rows(s).then_inc(S("dst_rows"), 1)
                pe.wait_ge(S("msg_eq"), i * 2 + 2)
                pe.wait_ge(S(f"gathered{s}"), i * 16 + (32 - 16 * s))
                if not (first and s == 0):
                    pe.wait_ge(S("msg_sums"), i)
                for a in range(2):
                    for b in range(2):
                        last = mm(BIG[0:TP, 0, a * 128:(a + 1) * 128], eq[:, s, b, a * TP:(a + 1) * TP], msg[:, s, b, :],
                                  b == 0, b == 1)
                last.then_inc(S("msg_used"), 1)
            pe.wait_ge(S("table_types_copied"), 1)
            pairs(pe, messages)
            pe.wait_ge(S("msg_sums"), NPAIR)
            to_feature_major([("agg_loaded", 16)])
            product([(adel, P0)], [("agg_scaled", 1)], "upd_out")
            layer_norm(7)
            to_node_major(X, [("x_final", 1)])

        @block.scalar
        def _(act):
            o = Order(act, S("act_order"))
            A_ = nc.scalar.activation
            nmr = [0]

            def copy_nm():
                nmr[0] += 1
                act.wait_ge(S("turned"), nmr[0] + turned_skip[0])
                o(A_(NM[:, :, :], bigT[0:TP, 0:NT, :], ACT.Copy))
                act.nop().then_inc(S("nm_ready"), 1)

            turned_skip = [0]

            def layer_norm(k):
                cen, sq = LN[k][1], LN[k][3]
                act.wait_ge(S("ln_cen"), k + 1)
                A_(sq, cen, ACT.Square).then_inc(S("ln_square"), 1)
                act.wait_ge(S("ln_var"), k + 1)
                A_(ch(LN[k][2]), big, ACT.Sqrt, bias=col("eps5")).then_inc(S("ln_std"), 1)

            def copy_slots(j):
                act.wait_ge(S("nm_ready"), (NM_V + NM_S)[j])

                def body(t, s, turn):
                    act.wait_ge(S("tile_free"), t + (NT * j + 1))
                    src_t = NM[:, t, :] if isinstance(t, int) else NM[:, bass.ds(t, 1), :].rearrange("p o n -> p (o n)")
                    A_(hs[:, s, :], src_t, ACT.Copy).then_inc(S("hs_ready"), 1)
                sweep(act, 2 + j, body)

            act.wait_ge(S("consts_made"), 1)
            layer_norm(0)
            for layer in range(2):
                act.wait_ge(S("gat_h"), layer + 1)
                A_(ch(H), big, ACT.Copy).then_inc(S("gat_h_copied"), 1)
                act.wait_ge(S("gat_s"), layer + 1)
                A_(ch(Sf), big, ACT.Copy).then_inc(S("gat_s_copied"), 1)
                act.wait_ge(S("gat_d"), layer + 1)
                A_(ch(Df), big, ACT.Copy).then_inc(S("gat_d_copied"), 1)
                turned_skip[0] += 1
                copy_nm()
                if layer == 0:
                    act.wait_ge(S("weights_loaded"), 16)
                    act.wait_ge(S("keys_made"), 1)

                    def build(i, s, first):
                        if not first:
                            act.wait_ge(S("edge_index"), i - 1)
                            act.wait_ge(S("edge_summed"), i - 1)
                        at = slice(2 * i, 2 * i + 2) if isinstance(i, int) else bass.ds(i * 2, 2)
                        A_(ks[:, s, :], keyF[:, at], ACT.Copy).then_inc(S("edge_slot"), 1)
                        A_(ws[:, s, :, 0], wF[:, at], ACT.Copy).then_inc(S("edge_slot"), 1)
                        act.wait_ge(S("edge_summed"), i + 1)
                        if not first:
                            act.wait_ge(S("counts_added"), i * 32 - 32)
                            act.wait_ge(S("weights_added"), i * 32 - 32)
                        A_(vs[:, s, :, :], SM[0:TP, 256:260].rearrange("p (a c) -> p a c", a=2), ACT.Copy).then_inc(S("edge_sums"), 1)
                    pairs(act, build)
                act.wait_ge(S("self_logit"), layer + 1)
                A_(P3, P3, ACT.Exp).then_inc(S("self_weight"), 1)

                def copy_rows(q):
                    if q >= 2:
                        act.wait_ge(S("u_made"), 25 * HEADS * (CH * layer + q - 1))
                    for k in range(2):
                        for h in range(HEADS):
                            n = ((layer * CH + q) * 2 + k) * HEADS + h
                            act.wait_ge(S("row_made"), n + 1)
                            A_(rows[:, q % 2, k, h, :], BIG[0:TP, 4 + h % 2, 0:CW], ACT.Copy).then_inc(S("row_copied"), 1)
                copy_rows(0)
                for q in range(CH):
                    if q + 1 < CH:
                        copy_rows(q + 1)
                    base = 25 * (CH * layer + q)

                    def body(t, s, turn):
                        for h in range(HEADS):
                            act.wait_ge(S("u_made"), t * HEADS + (HEADS * base + h + 1))
                            c = t * HEADS + h
                            sc = s2[:, c:c + 1] if isinstance(t, int) else s2[:, bass.ds(c, 1)]
                            A_(U[s][:, h, :], U[s][:, h, :], ACT.Exp, bias=sc).then_inc(S("exp_made"), 1)
                    sweep(act, CH * layer + q, body)
                    act.wait_ge(S("hp_free"), base + NT + 3)
                    A_(accs[:, :, :], BIG[:, 0:2, 0:CW], ACT.Copy).then_inc(S("acc_copied"), 1)
                    act.wait_ge(S("att_scaled"), layer * CH + q + 1)
                    A_(P1[:, q * CW:(q + 1) * CW], P1[:, q * CW:(q + 1) * CW], ACT.Relu,
                       bias=col("b1") if layer == 0 else col("b2")).then_inc(S("attended"), 1)
            layer_norm(1)
            act.wait_ge(S("norm2"), 1)
            A_(col("t1"), col("t0"), ACT.Sqrt).then_inc(S("norm2_root"), 1)
            for j in range(3):
                copy_nm()
                copy_slots(j)
                act.wait_ge(S("tile_free"), NT * (j + 1) + 3)
                A_(ch(P1), big, ACT.Copy).then_inc(S("agg_read"), 1)
                act.wait_ge(S("norm2"), j + 2)
                A_(col("t1"), col("t0"), ACT.Sqrt).then_inc(S("norm2_root"), 1)
            layer_norm(2)
            for j in range(3):
                copy_nm()
                copy_slots(3 + j)
                act.wait_ge(S("sage_out"), j + 1)
                A_(ch(P1), big, ACT.Identity, bias=col(f"sb{j + 1}")).then_inc(S("sage_biased"), 1)
                layer_norm(3 + j)
            layer_norm(6)
            act.wait_ge(S("w_turned"), 1)
            o(A_(asel, BIG[:, 0, 0:128], ACT.Copy))
            o(A_(adel, BIG[:, 1, 0:128], ACT.Copy))
            o(A_(weT[:, :], BIG[0:32, 2, 0:128], ACT.Copy))
            o(A_(embT[:, :], BIG[0:32, 3, 0:TYPES], ACT.Copy))
            act.nop().then_inc(S("w_copied"), 1)
            act.wait_ge(S("msg_x"), 1)
            o(A_(NM[:, :, :], bigT[0:TP, 0:NT, :], ACT.Copy))
            act.nop().then_inc(S("nm_ready"), 1)
            act.wait_ge(S("msg_t"), 1)
            A_(TR, bigT[0:TP, 0:TYPES, :], ACT.Copy).then_inc(S("table_types_copied"), 1)
            for k in range(TYPES):
                act.wait_ge(S("table_sum"), k + 1)
                if k >= 2:
                    act.wait_ge(S(f"table_out{k % 2}"), 16 * (k // 2))
                A_(tab[k % 2], tab[k % 2], ACT.Relu).then_inc(S("table_made"), 1)
            act.wait_ge(S("dst_made"), 1)

            def index_slot(i, s):
                at = slice(2 * i, 2 * i + 2) if isinstance(i, int) else bass.ds(i * 2, 2)
                A_(gs[:, s, :], gidx[:, at], ACT.Copy).then_inc(S("gather_index"), 1)

            index_slot(0, 0)
            index_slot(1, 1)

            def messages(i, s, first):
                if not first:
                    act.wait_ge(S("msg_index"), i - 1)
                at = slice(2 * i, 2 * i + 2) if isinstance(i, int) else bass.ds(i * 2, 2)
                A_(ks[:, s, :], keyF[:, at], ACT.Copy).then_inc(S("msg_slot"), 1)
                act.wait_ge(S(f"gathered{s}"), i * 16 + (32 - 16 * s))
                index_slot(i + 2, s)
                act.wait_ge(S("msg_used"), i + 1)
                if not first:
                    act.wait_ge(S("messages_added"), i * 32 - 32)
                A_(summed[:, s, :, :], BIG[0:TP, 0, 0:2 * D].rearrange("p (a n) -> p a n", a=2),
                   ACT.Copy).then_inc(S("msg_sums"), 1)
            pairs(act, messages)
            layer_norm(7)
            copy_nm()

        @block.vector
        def _(dve):
            v = nc.vector
            o = Order(dve, S("dve_order"))
            dve.nop().then_inc(S("seg_step"), 3 * HEADS)
            dve.nop().then_inc(S("w_made"), 3)

            def signal(name):
                dve.nop().then_inc(S(name), 1)

            def from_turned(op, result, other):
                q = N // 500 * 500
                for r, t, u in ((result[:, 0:q].rearrange("p (b n) -> p b n", n=500), BIG[:, 0:6, 0:500],
                                 other and other[:, 0:q].rearrange("p (b n) -> p b n", n=500)),
                                (result[:, q:N], BIG[:, 6, 0:N - q], other and other[:, q:N])):
                    o(v.tensor_copy(r, t) if other is None else v.tensor_tensor(r, t, u, op))

            def layer_norm(k, relu_to=None):
                src_arr, cen, dev, _ = LN[k]
                signal("ln_in")
                dve.wait_ge(S("ln_mean"), k + 1)
                v.tensor_tensor(ch(cen), ch(src_arr), big, ALU.subtract).then_inc(S("ln_cen"), 1)
                dve.wait_ge(S("ln_std"), k + 1)
                o(v.reciprocal(dev, dev))
                if relu_to is not None:
                    o(v.scalar_tensor_tensor(relu_to, cen, 0.0, dev, ALU.max, ALU.mult))
                else:
                    o(v.tensor_tensor(cen, cen, dev, ALU.mult))

            dve.wait_ge(S("consts_made"), 1)
            dve.wait_ge(S("params"), 16 * n_loads)
            dve.wait_ge(S("fm_turned"), 1)
            from_turned(None, X, None)
            layer_norm(0, H)
            signal("gat_in")

            def edge_steps(rows, used, index_ready, eq_done, writers, weights=False):
                def body(i, s, first):
                    dve.wait_ge(S(rows), i + 1)
                    if not first:
                        dve.wait_ge(S(used), i - 1)
                    for a in range(2):
                        v.tensor_scalar(eq[:, s, a, :], SM[0:TP, 0:2 * TP], ks[:, s, a:a + 1], None,
                                        ALU.is_equal).then_inc(S(eq_done), 1)
                    dve.wait_ge(S(eq_done), i * 2 + 2)
                    at = slice(2 * i, 2 * i + 2) if isinstance(i, int) else bass.ds(i * 2, 2)
                    for a in range(2):
                        o(v.tensor_tensor_reduce(eqo, eq[:, s, a, :], earlier[:, a, :], 1.0, 0.0, ALU.mult, ALU.add,
                                                 dup[:, s, a:a + 1]))
                    o(v.scalar_tensor_tensor(jk[:, s, :], dup[:, s, :], 1.0, junkD[:, at], ALU.min, ALU.mult))
                    if not first:
                        for w in writers:
                            dve.wait_ge(S(w), i * 32 - 32)
                    if weights:
                        o(v.scalar_tensor_tensor(jkw[:, s, :], dup[:, s, :], 1.0, junkW[:, at], ALU.min, ALU.mult))
                        o(v.tensor_tensor(idxw[:, s, :], jkw[:, s, :], keyW[:, at], ALU.add))
                    v.tensor_tensor(idx[:, s, :], jk[:, s, :], ks[:, s, :], ALU.add).then_inc(S(index_ready), 1)
                pairs(dve, body, o, 5 if weights else 3)

            def junk_steps(at, junk=junkD, key=keyF):
                for a in range(2):
                    cut = slice(a, EC, 2)
                    o(v.tensor_scalar(junk[:, cut], key[:, cut], -1.0, junk_f[:, at + a:at + a + 1], ALU.mult, ALU.add))

            for layer in range(2):
                o(v.tensor_scalar(asel, block_m, col("as1" if layer == 0 else "as2"), None, ALU.mult))
                o(v.tensor_scalar(adel, block_m, col("ad1" if layer == 0 else "ad2"), None, ALU.mult))
                signal("gat_sel")
                dve.wait_ge(S("turned"), 2 * layer + 1)
                o(v.tensor_copy(s1[:, :].rearrange("p (t h) -> p t h", h=HEADS),
                                bigT[0:TP, 0:NT, :].rearrange("p t (h c) -> p t h c", c=HC)[:, :, :, 0]))
                o(v.tensor_scalar(s8[:, :], s1[:, :], 0.8, None, ALU.mult))
                o(v.tensor_scalar(s2[:, :], s1[:, :], 0.2, None, ALU.mult))
                signal("s_cols")
                if layer == 0:
                    o(v.tensor_copy(junk_f[:, :], junk_i[:, :]))
                    o(v.tensor_copy(keyF, dstI))
                    o(v.scalar_tensor_tensor(keyF, srcI, float(NP), keyF, ALU.mult, ALU.add))
                    junk_steps(0)
                    o(v.tensor_copy(keyW, srcI))
                    o(v.scalar_tensor_tensor(keyW, dstI, float(NP), keyW, ALU.mult, ALU.add))
                    junk_steps(0, junkW, keyW)
                    signal("keys_made")
                    edge_steps("key_rows", "edge_summed", "edge_index", "edge_eq", ("weights_added", "counts_added"), True)
                    dve.wait_ge(S("count_done"), 1)
                def body(t, s, turn):
                    dve.wait_ge(S("mask_made"), t + (NT * layer + 1))
                    for h in range(HEADS):
                        if isinstance(t, int) and t == 0:
                            v.tensor_scalar(seg[:, h, :], A[s], s1[:, h:h + 1], None, ALU.add).then_inc(S("seg_step"), 1)
                            continue
                        c = t * HEADS + h
                        sc = s1[:, c:c + 1] if isinstance(t, int) else s1[:, bass.ds(c, 1)]
                        dve.wait_ge(S("seg_step"), t * HEADS + (HEADS * NT * layer + h + 1 - HEADS + 3 * HEADS))
                        v.scalar_tensor_tensor(seg[:, h, :], A[s], sc, seg[:, h, :], ALU.add, ALU.max).then_inc(S("seg_step"), 1)
                sweep(dve, layer, body)
                if layer == 0:
                    dve.wait_ge(S("deg_used"), NT)
                    o(v.tensor_scalar(ch(Dinv), big, 1.0, None, ALU.max))
                    signal("deg_read")
                    o(v.reciprocal(Dinv, Dinv))
                for t in range(NT):
                    dve.wait_ge(S("seg_turned"), NT * layer + t + 1)
                    v.tensor_reduce(smax[:, t, :], BIG[0:TP, t % CH, 0:HEADS * TP].rearrange("p (h n) -> p h n", h=HEADS),
                                    AX.X, ALU.max).then_inc(S("smax_made"), 1)
                dve.wait_ge(S("smax_made"), NT * (layer + 1))
                v.tensor_copy(smaxD.rearrange("p (n c) -> p n c", c=HC),
                              smax[:, :, :].rearrange("p t h -> p (t h)").unsqueeze(2).to_broadcast([TP, NT * HEADS, HC])
                              ).then_inc(S("smax_spread"), 1)
                dve.wait_ge(S("smax_turned"), layer + 1)
                from_turned(ALU.max, P0, Sf)
                o(v.tensor_copy(P0[:, N:NP], Sf[:, N:NP]))
                o(v.tensor_tensor(P0, P0, Df, ALU.add))
                o(v.scalar_tensor_tensor(P0, P0, 0.2, P0, ALU.mult, ALU.max))
                o(v.tensor_tensor(P1, Df, P0, ALU.subtract))
                o(v.scalar_tensor_tensor(P2, Df, 0.2, P0, ALU.mult, ALU.subtract))
                o(v.tensor_tensor(P3, Sf, Df, ALU.add))
                o(v.scalar_tensor_tensor(P3, P3, 0.2, P3, ALU.mult, ALU.max))
                o(v.tensor_tensor(P3, P3, P0, ALU.subtract))
                signal("self_logit")
                signal("gat_rows")
                dve.wait_ge(S("self_weight"), layer + 1)
                for q in range(CH):
                    n = CH * layer + q
                    base = NT * n

                    def logits(t, s):
                        dve.wait_ge(S("hp_free"), t + (base + 1))
                        for h in range(HEADS):
                            c = t * HEADS + h
                            sc = s8[:, c:c + 1] if isinstance(t, int) else s8[:, bass.ds(c, 1)]
                            v.scalar_tensor_tensor(U[s][:, h, :], rows[:, q % 2, 0, h, :], sc, rows[:, q % 2, 1, h, :],
                                                   ALU.add, ALU.max).then_inc(S("u_made"), 1)

                    def body(t, s, turn):
                        if not (isinstance(t, int) and t == NT - 1):
                            logits(t + 1, (s + 1) % 3)
                        dve.wait_ge(S("exp_made"), t * HEADS + (HEADS * base + HEADS))
                        dve.wait_ge(S(f"block_in{s}"), (turn + 1) * 16)
                        v.tensor_tensor(U[s], U[s], B[s].unsqueeze(1).to_broadcast([TP, HEADS, CW]),
                                        ALU.mult).then_inc(S("w_made"), 1)

                    dve.wait_ge(S("row_copied"), 2 * HEADS * (n + 1))
                    logits(0, base % 3)
                    sweep(dve, n, body)
                    cut = slice(q * CW, (q + 1) * CW)
                    dve.wait_ge(S("att_placed"), n + 1)
                    o(v.tensor_tensor(P2[:, cut], P3[:, cut], H[:, cut], ALU.mult))
                    o(v.tensor_tensor(P2[:, cut], P2[:, cut], BIG[:, 2, 0:CW], ALU.add))
                    o(v.tensor_tensor(P3[:, cut], P3[:, cut], BIG[:, 3, 0:CW], ALU.add))
                    o(v.tensor_scalar(P3[:, cut], P3[:, cut], 1e-16, None, ALU.max))
                    o(v.reciprocal(P3[:, cut], P3[:, cut]))
                    v.tensor_tensor(P1[:, cut], P2[:, cut], P3[:, cut], ALU.mult).then_inc(S("att_scaled"), 1)
            dve.wait_ge(S("attended"), 2 * CH)
            o(v.tensor_tensor(X, X, P1, ALU.add))

            layer_norm(1, H)

            def square_sum(a, b, to):
                o(v.tensor_tensor_reduce(P2[:, 0:N], a[:, 0:N], b[:, 0:N], 1.0, 0.0, ALU.mult, ALU.add, col(to)))

            square_sum(H, H, "t0")
            o(v.tensor_scalar(col("t0"), col("t0"), 1e-12, None, ALU.max))
            signal("norm2")
            dve.wait_ge(S("norm2_root"), 1)
            o(v.reciprocal(col("t2"), col("t1")))
            o(v.tensor_scalar(H, H, col("t2"), None, ALU.mult))
            signal("v_ready")
            for j in range(3):
                dve.wait_ge(S("agg_read"), j + 1)
                square_sum(P1, V[j], "alpha")
                o(v.tensor_scalar(col("alpha"), col("alpha"), -1.0, None, ALU.mult))
                o(v.scalar_tensor_tensor(P1, V[j], col("alpha"), P1, ALU.mult, ALU.add))
                if j:
                    o(v.scalar_tensor_tensor(P1, V[j - 1], col("nbeta"), P1, ALU.mult, ALU.add))
                square_sum(P1, P1, "t0")
                signal("norm2")
                dve.wait_ge(S("norm2_root"), j + 2)
                o(v.tensor_scalar(col("nbeta"), col("t1"), -1.0, None, ALU.mult))
                o(v.reciprocal(col("t2"), col("t1")))
                o(v.tensor_scalar(V[j + 1], P1, col("t2"), None, ALU.mult))
                signal("v_ready")
            dve.wait_ge(S("lanczos_out"), 1)
            o(v.scalar_tensor_tensor(ch(X), big, 0.0, ch(X), ALU.max, ALU.add))

            layer_norm(2, H)
            for j in range(3):
                if j == 1:
                    dve.wait_ge(S("skip"), 1)
                    o(v.tensor_tensor(ch(Df), big, ch(Sf), ALU.add))
                if j == 2:
                    o(v.tensor_tensor(Sf, Sf, Df, ALU.add))
                    dve.wait_ge(S("skip"), 2)
                    o(v.tensor_tensor(ch(Sf), big, ch(Sf), ALU.add))
                signal("sage_in")
                dve.wait_ge(S("tile_free"), NT * (4 + j) + 3)
                o(v.tensor_tensor(ch(P0), big, ch(Dinv), ALU.mult))
                signal("sage_agg")
                dve.wait_ge(S("sage_biased"), j + 1)
                layer_norm(3 + j)
                o(v.tensor_scalar(P2, P2, col(f"g{j + 1}"), col(f"beta{j + 1}"), ALU.mult, ALU.add))
                o(v.tensor_scalar(P3, P2, 0.0, col(f"a{j + 1}"), ALU.min, ALU.mult))
                o(v.scalar_tensor_tensor((Sf, Df, P2)[j], P2, 0.0, P3, ALU.max, ALU.add))
                signal("sage_prev")
            o(v.tensor_tensor(X, X, P2, ALU.add))

            layer_norm(6, H)
            signal("h3_ready")
            o(v.tensor_copy(keyF, dstI))
            junk_steps(2)
            o(v.memset(gidx[:, EC:EC + 4], 0))
            o(v.scalar_tensor_tensor(gidx[:, 0:EC], typeI, float(N), srcI, ALU.mult, ALU.add))
            signal("dst_made")
            dve.wait_ge(S("nm_ready"), NM_MSG)
            dve.wait_ge(S("table_types_copied"), 1)
            for k in range(TYPES):
                if k >= 2:
                    dve.wait_ge(S(f"table_out{k % 2}"), 16 * (k // 2))
                v.tensor_tensor(tab[k % 2], NM[:, :, :], TR[:, k, :].unsqueeze(1).to_broadcast([TP, NT, D]),
                                ALU.add).then_inc(S("table_sum"), 1)
            edge_steps("dst_rows", "msg_used", "msg_index", "msg_eq", ("messages_added",))
            dve.wait_ge(S("fm_turned"), 2)
            from_turned(ALU.mult, P0, Dinv)
            o(v.memset(P0[:, N:NP], 0.0))
            signal("agg_scaled")
            dve.wait_ge(S("upd_out"), 1)
            o(v.scalar_tensor_tensor(ch(P1), big, col("updb"), ch(H), ALU.add, ALU.add))
            layer_norm(7)
            o(v.tensor_scalar(P2, P2, col("lng"), col("lnb"), ALU.mult, ALU.add))
            o(v.tensor_tensor(X, X, P2, ALU.add))
            signal("x_final")


_INS = ['x', 'src', 'dst', 'edge_type_16', 'edge_weight', 'L0_gnn_W1', 'L0_gnn_a_src1', 'L0_gnn_a_dst1',
        'L0_gnn_b1', 'L0_gnn_W2', 'L0_gnn_a_src2', 'L0_gnn_a_dst2', 'L0_gnn_b2', 'L1_gnn_weights',
        'L2_gnn_Wself1', 'L2_gnn_Wneigh1', 'L2_gnn_b1', 'L2_gnn_Wself2', 'L2_gnn_Wneigh2', 'L2_gnn_b2',
        'L2_gnn_Wself3', 'L2_gnn_Wneigh3', 'L2_gnn_b3', 'L2_gnn_Wskip1', 'L2_gnn_Wskip2', 'L2_gnn_g1',
        'L2_gnn_beta1', 'L2_gnn_g2', 'L2_gnn_beta2', 'L2_gnn_g3', 'L2_gnn_beta3', 'L2_gnn_a1', 'L2_gnn_a2',
        'L2_gnn_a3', 'L3_gnn_edge_emb_W', 'L3_gnn_msg_W', 'L3_gnn_msg_b', 'L3_gnn_upd_W', 'L3_gnn_upd_b',
        'L3_gnn_ln_g', 'L3_gnn_ln_b']


def kernel(**inputs):
    import numpy as _np
    import concourse.bacc as _bacc
    from concourse import mybir as _mybir
    from concourse.bass_utils import run_bass_kernel_spmd as _run

    nc = _bacc.Bacc("TRN2", target_bir_lowering=False, num_devices=1)
    arrays, args = {}, []
    for name in _INS:
        a = _np.ascontiguousarray(inputs[name])
        if a.ndim == 0:
            a = a.reshape(1)
        arrays[f"in_{name}_dram"] = a
        args.append(nc.dram_tensor(f"in_{name}_dram", a.shape, _mybir.dt.from_np(a.dtype), kind="ExternalInput").ap())
    args.append(nc.dram_tensor("out_0_dram", (N, D), _mybir.dt.float32, kind="ExternalOutput").ap())
    graph_layers(nc, *args)
    r = _run(nc, [arrays], core_ids=[0])
    return r.results[0]["out_0_dram"]
```
